# Optimizing a Trainium2 kernel written in Bass

```python
import numpy as np
import jax
import jax.numpy as jnp

def _softmax(x, axis=-1):
    return jax.nn.softmax(x, axis=axis)

def _gelu(x):
    return jax.nn.gelu(x, approximate=True)

def _silu(x):
    return jax.nn.silu(x)

def _sigmoid(x):
    return jax.nn.sigmoid(x)

def _layernorm(x, axis=-1, eps=1e-05):
    m = jnp.mean(x, axis=axis, keepdims=True)
    v = jnp.var(x, axis=axis, keepdims=True)
    return (x - m) / jnp.sqrt(v + eps)

def _scatter_add(tgt, idx, src, axis=0):
    return tgt.at[idx].add(src)

def _segment_sum(src, seg, n):
    return jax.ops.segment_sum(src, seg, n)
kernel_name = 'mk_seq_preln_d2_jaxref_r4_01159b'

def setup_inputs(seed: int=0):
    np.random.seed(seed)
    _w = jnp.asarray

    def _L0_attn_setup():
        import jax, jax.numpy as jnp
        import numpy as np
        import math
        B, S, E = (2, 512, 256)
        H, DC, DR = (16, 64, 128)
        HD = E // H

        def _linear_params(key, din, dout):
            k1, k2 = jax.random.split(key)
            bound = 1.0 / math.sqrt(din)
            w = jax.random.uniform(k1, (din, dout), minval=-bound, maxval=bound, dtype=jnp.float32)
            b = jax.random.uniform(k2, (dout,), minval=-bound, maxval=bound, dtype=jnp.float32)
            return (w, b)

        def _gelu(x):
            return jax.nn.gelu(x, approximate=False)

        def _rope_cos_sin(seq_len, d_rope):
            inv_freq = 1.0 / 10000.0 ** (jnp.arange(0, d_rope, 2, dtype=jnp.float32) / d_rope)
            t = jnp.arange(seq_len, dtype=jnp.float32)
            freqs = t[:, None] * inv_freq[None, :]
            emb = jnp.concatenate([freqs, freqs], axis=-1)
            return (jnp.cos(emb), jnp.sin(emb))

        def _apply_rope(x, cos, sin):
            d = x.shape[-1]
            x1, x2 = (x[..., :d // 2], x[..., d // 2:])
            rot = jnp.concatenate([-x2, x1], axis=-1)
            return x * cos + rot * sin
        key = jax.random.key(seed)
        ks = jax.random.split(key, 10)
        x = jax.random.normal(ks[0], (B, S, E), dtype=jnp.float32)
        wq, bq = _linear_params(ks[1], E, DC)
        wqc, bqc = _linear_params(ks[2], DC, E - DR)
        wqr, bqr = _linear_params(ks[3], E, DR)
        wkv, bkv = _linear_params(ks[4], E, DC)
        wkr, bkr = _linear_params(ks[5], E, DR)
        wkc, bkc = _linear_params(ks[6], DC, E - DR)
        wv, bv = _linear_params(ks[7], DC, E)
        wo, bo = _linear_params(ks[8], E, E)
        return dict(x=x, wq=wq, bq=bq, wqc=wqc, bqc=bqc, wqr=wqr, bqr=bqr, wkv=wkv, bkv=bkv, wkr=wkr, bkr=bkr, wkc=wkc, bkc=bkc, wv=wv, bv=bv, wo=wo, bo=bo)
    _L0_attn_in = _L0_attn_setup()

    def _L0_ffn_setup():
        import jax, jax.numpy as jnp
        import numpy as np
        from jax import lax
        H = 256
        E = 8
        E_MLP = E - 4
        TOP_K = 2
        I = 128
        KC = 4
        SHARED_SCALE = 1.0
        key = jax.random.key(seed)
        ks = jax.random.split(key, 8)
        B, S = (4, 1024)
        s_h = 1.0 / np.sqrt(H)
        s_i = 1.0 / np.sqrt(I)
        return {'hidden_states': jax.random.normal(ks[0], (B, S, H), dtype=jnp.float32), 'Wr': jax.random.normal(ks[1], (H, E), dtype=jnp.float32) * s_h, 'router_bias': jnp.zeros((E,), dtype=jnp.float32), 'Wg': jax.random.normal(ks[2], (E_MLP, H, I), dtype=jnp.float32) * s_h, 'Wu': jax.random.normal(ks[3], (E_MLP, H, I), dtype=jnp.float32) * s_h, 'Wd': jax.random.normal(ks[4], (E_MLP, I, H), dtype=jnp.float32) * s_i, 'conv_w': jax.random.normal(ks[5], (KC, 1, H), dtype=jnp.float32) * (1.0 / np.sqrt(KC)), 'conv_b': jnp.zeros((H,), dtype=jnp.float32)}
    _L0_ffn_in = _L0_ffn_setup()

    def _L1_attn_setup():
        import jax, jax.numpy as jnp
        import numpy as np
        EMBED = 256
        HEADS = 16
        HEAD_DIM = EMBED // HEADS
        key = jax.random.key(seed)
        k1, k2, k3, k4, k5 = jax.random.split(key, 5)
        s = 1.0 / np.sqrt(EMBED)
        return {'x': jax.random.normal(k1, (4, 512, EMBED), dtype=jnp.float32), 'Wqkv': jax.random.uniform(k2, (EMBED, 3 * EMBED), jnp.float32, -s, s), 'bqkv': jax.random.uniform(k3, (3 * EMBED,), jnp.float32, -s, s), 'Wo': jax.random.uniform(k4, (EMBED, EMBED), jnp.float32, -s, s), 'bo': jax.random.uniform(k5, (EMBED,), jnp.float32, -s, s)}
    _L1_attn_in = _L1_attn_setup()

    def _L1_ffn_setup():
        import jax, jax.numpy as jnp
        import numpy as np

        def gelu(x):
            return jax.nn.gelu(x, approximate=False)
        key = jax.random.key(seed)
        ks = jax.random.split(key, 6)
        B, S, d_model = (4, 512, 256)
        n_input, n_process, n_output, d_pv = (2048, 1024, 2048, 128)
        s = 0.02
        return {'x': jax.random.normal(ks[0], (B, S, d_model), jnp.float32), 'input_patterns': jax.random.normal(ks[1], (n_input, d_model), jnp.float32) * s, 'process_input_weights': jax.random.normal(ks[2], (n_process, n_input), jnp.float32) * s, 'process_values': jax.random.normal(ks[3], (n_process, d_pv), jnp.float32) * s, 'output_input_weights': jax.random.normal(ks[4], (n_output, d_pv), jnp.float32) * s, 'output_patterns': jax.random.normal(ks[5], (n_output, d_model), jnp.float32) * s}
    _L1_ffn_in = _L1_ffn_setup()
    _d = {'L0_attn_x': _L0_attn_in['x'], 'L0_attn_wq': _L0_attn_in['wq'], 'L0_attn_bq': _L0_attn_in['bq'], 'L0_attn_wqc': _L0_attn_in['wqc'], 'L0_attn_bqc': _L0_attn_in['bqc'], 'L0_attn_wqr': _L0_attn_in['wqr'], 'L0_attn_bqr': _L0_attn_in['bqr'], 'L0_attn_wkv': _L0_attn_in['wkv'], 'L0_attn_bkv': _L0_attn_in['bkv'], 'L0_attn_wkr': _L0_attn_in['wkr'], 'L0_attn_bkr': _L0_attn_in['bkr'], 'L0_attn_wkc': _L0_attn_in['wkc'], 'L0_attn_bkc': _L0_attn_in['bkc'], 'L0_attn_wv': _L0_attn_in['wv'], 'L0_attn_bv': _L0_attn_in['bv'], 'L0_attn_wo': _L0_attn_in['wo'], 'L0_attn_bo': _L0_attn_in['bo'], 'L0_ffn_Wr': _L0_ffn_in['Wr'], 'L0_ffn_router_bias': _L0_ffn_in['router_bias'], 'L0_ffn_Wg': _L0_ffn_in['Wg'], 'L0_ffn_Wu': _L0_ffn_in['Wu'], 'L0_ffn_Wd': _L0_ffn_in['Wd'], 'L0_ffn_conv_w': _L0_ffn_in['conv_w'], 'L0_ffn_conv_b': _L0_ffn_in['conv_b'], 'L1_attn_Wqkv': _L1_attn_in['Wqkv'], 'L1_attn_bqkv': _L1_attn_in['bqkv'], 'L1_attn_Wo': _L1_attn_in['Wo'], 'L1_attn_bo': _L1_attn_in['bo'], 'L1_ffn_input_patterns': _L1_ffn_in['input_patterns'], 'L1_ffn_process_input_weights': _L1_ffn_in['process_input_weights'], 'L1_ffn_process_values': _L1_ffn_in['process_values'], 'L1_ffn_output_input_weights': _L1_ffn_in['output_input_weights'], 'L1_ffn_output_patterns': _L1_ffn_in['output_patterns']}
    _x0 = _d['L0_attn_x']
    _d['L0_attn_x'] = jax.random.normal(jax.random.fold_in(jax.random.key(seed), 1), (32, 512, 256), dtype=_x0.dtype)
    del _x0
    return _d

def reference(L0_attn_x, L0_attn_wq, L0_attn_bq, L0_attn_wqc, L0_attn_bqc, L0_attn_wqr, L0_attn_bqr, L0_attn_wkv, L0_attn_bkv, L0_attn_wkr, L0_attn_bkr, L0_attn_wkc, L0_attn_bkc, L0_attn_wv, L0_attn_bv, L0_attn_wo, L0_attn_bo, L0_ffn_Wr, L0_ffn_router_bias, L0_ffn_Wg, L0_ffn_Wu, L0_ffn_Wd, L0_ffn_conv_w, L0_ffn_conv_b, L1_attn_Wqkv, L1_attn_bqkv, L1_attn_Wo, L1_attn_bo, L1_ffn_input_patterns, L1_ffn_process_input_weights, L1_ffn_process_values, L1_ffn_output_input_weights, L1_ffn_output_patterns):

    def _L0_attn_ref(x, wq, bq, wqc, bqc, wqr, bqr, wkv, bkv, wkr, bkr, wkc, bkc, wv, bv, wo, bo):
        import jax, jax.numpy as jnp
        import numpy as np
        import math
        B, S, E = (2, 512, 256)
        H, DC, DR = (16, 64, 128)
        HD = E // H

        def _linear_params(key, din, dout):
            k1, k2 = jax.random.split(key)
            bound = 1.0 / math.sqrt(din)
            w = jax.random.uniform(k1, (din, dout), minval=-bound, maxval=bound, dtype=jnp.float32)
            b = jax.random.uniform(k2, (dout,), minval=-bound, maxval=bound, dtype=jnp.float32)
            return (w, b)

        def _gelu(x):
            return jax.nn.gelu(x, approximate=False)

        def _rope_cos_sin(seq_len, d_rope):
            inv_freq = 1.0 / 10000.0 ** (jnp.arange(0, d_rope, 2, dtype=jnp.float32) / d_rope)
            t = jnp.arange(seq_len, dtype=jnp.float32)
            freqs = t[:, None] * inv_freq[None, :]
            emb = jnp.concatenate([freqs, freqs], axis=-1)
            return (jnp.cos(emb), jnp.sin(emb))

        def _apply_rope(x, cos, sin):
            d = x.shape[-1]
            x1, x2 = (x[..., :d // 2], x[..., d // 2:])
            rot = jnp.concatenate([-x2, x1], axis=-1)
            return x * cos + rot * sin
        b, s, _ = x.shape
        cq = _gelu(x @ wq + bq)
        q_c = cq @ wqc + bqc
        q_r = x @ wqr + bqr
        ckv = _gelu(x @ wkv + bkv)
        k_r = x @ wkr + bkr
        k_c = ckv @ wkc + bkc
        v = (ckv @ wv + bv).reshape(b, s, H, HD).transpose(0, 2, 1, 3)
        cos, sin = _rope_cos_sin(s, DR)
        q_r = _apply_rope(q_r, cos, sin)
        k_r = _apply_rope(k_r, cos, sin)
        q = _gelu(jnp.concatenate([q_c, q_r], axis=-1)).reshape(b, s, H, HD).transpose(0, 2, 1, 3)
        k = _gelu(jnp.concatenate([k_c, k_r], axis=-1)).reshape(b, s, H, HD).transpose(0, 2, 1, 3)
        scale = 1.0 / math.sqrt(HD)
        scores = jnp.einsum('bhqd,bhkd->bhqk', q, k) * scale
        causal = jnp.triu(jnp.ones((s, s), dtype=bool), k=1)
        scores = jnp.where(causal[None, None], -jnp.inf, scores)
        attn = jax.nn.softmax(scores, axis=-1)
        out = jnp.einsum('bhqk,bhkd->bhqd', attn, v)
        out = out.transpose(0, 2, 1, 3).reshape(b, s, E)
        return out @ wo + bo

    def _L0_ffn_ref(hidden_states, Wr, router_bias, Wg, Wu, Wd, conv_w, conv_b):
        import jax, jax.numpy as jnp
        import numpy as np
        from jax import lax
        H = 256
        E = 8
        E_MLP = E - 4
        TOP_K = 2
        I = 128
        KC = 4
        SHARED_SCALE = 1.0
        B, S, Hd = hidden_states.shape
        T = B * S
        x = hidden_states.reshape(T, Hd)
        scores = jax.nn.sigmoid(x @ Wr)
        _, idx = lax.top_k(scores + router_bias, TOP_K)
        w = jnp.take_along_axis(scores, idx, axis=-1)
        w = w / (jnp.sum(w, axis=-1, keepdims=True) + 1e-09)
        cw = jnp.zeros((T, E), dtype=x.dtype).at[jnp.arange(T)[:, None], idx].add(w)
        g = jnp.einsum('th,ehi->tei', x, Wg)
        u = jnp.einsum('th,ehi->tei', x, Wu)
        hid = jax.nn.silu(g) * u
        mlp_out = jnp.einsum('tei,eih->teh', hid, Wd)
        routed = jnp.einsum('te,teh->th', cw[:, :E_MLP], mlp_out)
        routed = routed + cw[:, E_MLP:E_MLP + 1] * x
        routed = routed + cw[:, E_MLP + 2:E_MLP + 3] * x
        routed = routed + cw[:, E_MLP + 3:E_MLP + 4] * jax.nn.relu(x)
        routed = routed.reshape(B, S, Hd)
        shared = lax.conv_general_dilated(hidden_states, conv_w, window_strides=(1,), padding=[(KC - 1, 0)], dimension_numbers=('NHC', 'HIO', 'NHC'), feature_group_count=Hd) + conv_b
        return routed + SHARED_SCALE * shared

    def _L1_attn_ref(x, Wqkv, bqkv, Wo, bo):
        import jax, jax.numpy as jnp
        import numpy as np
        EMBED = 256
        HEADS = 16
        HEAD_DIM = EMBED // HEADS
        B, S, E = x.shape
        qkv = x @ Wqkv + bqkv
        qkv = qkv.reshape(B, S, 3, HEADS, HEAD_DIM)
        qkv = jnp.transpose(qkv, (2, 0, 3, 1, 4))
        q, k, v = (qkv[0], qkv[1], qkv[2])
        scale = 1.0 / np.sqrt(HEAD_DIM).astype(np.float32)
        scores = jnp.einsum('bhqd,bhkd->bhqk', q, k) * scale
        attn = jax.nn.softmax(scores, axis=-1)
        out = jnp.einsum('bhqk,bhkd->bhqd', attn, v)
        out = jnp.transpose(out, (0, 2, 1, 3)).reshape(B, S, E)
        return out @ Wo + bo

    def _L1_ffn_ref(x, input_patterns, process_input_weights, process_values, output_input_weights, output_patterns):
        import jax, jax.numpy as jnp
        import numpy as np

        def gelu(x):
            return jax.nn.gelu(x, approximate=False)
        B, S, d_model = x.shape
        n_input = input_patterns.shape[0]
        n_process = process_input_weights.shape[0]
        n_output = output_input_weights.shape[0]
        k_input = max(n_input // 8, 64)
        k_process = max(n_process // 8, 32)
        k_output = max(n_output // 8, 64)
        input_acts = gelu(jnp.einsum('bsd,nd->bsn', x, input_patterns))
        input_acts_seq = input_acts.mean(axis=1)
        top_input_acts, top_input_idx = jax.lax.top_k(input_acts_seq, k_input)
        brow = jnp.arange(B)[:, None]
        input_repr = jnp.zeros((B, n_input), x.dtype).at[brow, top_input_idx].set(top_input_acts)
        process_acts = gelu(jnp.einsum('bn,pn->bp', input_repr, process_input_weights))
        top_process_acts, top_process_idx = jax.lax.top_k(process_acts, k_process)
        selected_process_values = process_values[top_process_idx]
        process_weights = jax.nn.softmax(top_process_acts, axis=-1)
        aggregated_value = jnp.einsum('bk,bkd->bd', process_weights, selected_process_values)
        output_acts_seq = gelu(jnp.einsum('bd,od->bo', aggregated_value, output_input_weights))
        top_output_acts, top_output_idx = jax.lax.top_k(output_acts_seq, k_output)
        selected_output_patterns = output_patterns[top_output_idx]
        out_per_seq = jnp.einsum('bk,bkm->bm', top_output_acts, selected_output_patterns)
        output = jnp.broadcast_to(out_per_seq[:, None, :], (B, S, d_model))
        return output
    x = L0_attn_x
    x = x + _L0_attn_ref(_layernorm(x, axis=-1), L0_attn_wq, L0_attn_bq, L0_attn_wqc, L0_attn_bqc, L0_attn_wqr, L0_attn_bqr, L0_attn_wkv, L0_attn_bkv, L0_attn_wkr, L0_attn_bkr, L0_attn_wkc, L0_attn_bkc, L0_attn_wv, L0_attn_bv, L0_attn_wo, L0_attn_bo)
    x = x + _L0_ffn_ref(_layernorm(x, axis=-1), L0_ffn_Wr, L0_ffn_router_bias, L0_ffn_Wg, L0_ffn_Wu, L0_ffn_Wd, L0_ffn_conv_w, L0_ffn_conv_b)
    x = x + _L1_attn_ref(_layernorm(x, axis=-1), L1_attn_Wqkv, L1_attn_bqkv, L1_attn_Wo, L1_attn_bo)
    x = x + _L1_ffn_ref(_layernorm(x, axis=-1), L1_ffn_input_patterns, L1_ffn_process_input_weights, L1_ffn_process_values, L1_ffn_output_input_weights, L1_ffn_output_patterns)
    return x

_drawn_inputs = setup_inputs


def setup_inputs(seed=0):
    import zlib

    import numpy as np

    out = dict(_drawn_inputs(seed))
    spreads = {'L0_ffn_router_bias': (0.0, 0.1), 'L0_ffn_conv_b': (0.0, 0.1)}
    factors = {'L0_attn_wq': 8.0,
     'L0_attn_bq': 8.0,
     'L0_attn_wqc': 8.0,
     'L0_attn_bqc': 8.0,
     'L0_attn_wqr': 8.0,
     'L0_attn_bqr': 8.0,
     'L0_attn_bkv': 2.839,
     'L0_attn_wkr': 8.0,
     'L0_attn_bkr': 8.0,
     'L0_attn_wkc': 8.0,
     'L0_attn_bkc': 8.0,
     'L1_attn_Wqkv': 3.081,
     'L1_attn_bqkv': 3.99,
     'L1_attn_bo': 2.686,
     'L1_ffn_input_patterns': 8.0,
     'L1_ffn_process_input_weights': 8.0,
     'L1_ffn_process_values': 8.0,
     'L1_ffn_output_input_weights': 8.0,
     'L1_ffn_output_patterns': 8.0}
    for name, (base, spread) in spreads.items():
        noise = np.random.default_rng([zlib.crc32(name.encode()), seed]).standard_normal(out[name].shape)
        drawn = base * np.exp(spread * noise) if base else spread * noise
        out[name] = jnp.asarray(drawn.astype(out[name].dtype))
    for name, factor in factors.items():
        out[name] = (out[name] * factor).astype(out[name].dtype)
    return out
```

```python
from contextlib import ExitStack

import numpy as np

import concourse.bass as bass
from concourse import mybir

F32 = mybir.dt.float32
F32R = mybir.dt.float32r
BF16 = mybir.dt.bfloat16
ALU = mybir.AluOpType
ACT = mybir.ActivationFunctionType
AX = mybir.AxisListType

P = 128
B, S, E = 32, 512, 256
H, HD = 16, 16
TT = S // P
CC = E // P
HH = H // 2
SCALE = 1.0 / HD ** 0.5
EPS = 1e-5
NEXP = 4
NE = 8
INNER = 128
TAPS = 4
N_IN, N_PROC, N_OUT, D_PV = 2048, 1024, 2048, 128
K_IN, K_PROC, K_OUT = N_IN // 8, N_PROC // 8, N_OUT // 8
FT = N_IN // P
BLK = 3 * HD
SHIFT = 2 * BLK
STACK = SHIFT + 2
VW = HD + 1
MASKED = -1e30
LOWEST = -3.0e38
SEM_DMA = 16

_AT = 0


def _cols(n):
    global _AT
    _AT += n
    return _AT - n


W_C = _cols(CC * P)
W_QR = _cols(CC * P)
W_QS = _cols(CC * P)
W_KR = _cols(CC * P)
W_KS = _cols(CC * P)
W_QC = _cols(P)
W_KC = _cols(P)
W_V0 = _cols(E)
W_O0 = _cols(CC * E)
W_QK1 = _cols(CC * 2 * E)
W_V1 = _cols(CC * E)
W_O1 = _cols(CC * E)
W_GU = _cols(CC * NEXP * 2 * INNER)
W_D = _cols(NEXP * E)
W_R = _cols(CC * NE)
W_COLS = _AT
W_PARTS = 2

(C_BC, C_BQC, C_BKC, C_BQR, C_BQS, C_BKR, C_BKS, C_BQ1, C_BK1, C_CW, C_CB) = (0, 1, 2, 3, 4, 5, 6, 7, 9, 11, 19)
C_COLS = 21
R_BV0, R_BO0, R_BV1, R_BO1, R_BR, R_REV = 0, 256, 512, 768, 1024, 1056
R_COLS = 1088

BANKS = 7


def attention_items():
    s = [[("s", hf, hh, qt) for hh in range(HH) for qt in range(TT)] for hf in range(2)]

    def units(hf):
        order = [(g, kt) for g in range(HH // 4) for kt in range(TT)]
        out = []
        for n, (g, kt) in enumerate(order):
            out.append([("t", hf, g, kt, j) for j in range(4)])
            if n:
                out[-1].append(("pv", hf, *order[n - 1]))
        out[-1].append(("pv", hf, *order[-1]))
        return out

    items = s[0] + [("m", 0)] + s[1][:8]
    for n, unit in enumerate(units(0)):
        items += unit + s[1][8 + 3 * n:11 + 3 * n]
    items.append(("m", 1))
    for unit in units(1):
        items += unit
    return items


ITEMS = attention_items()


def ring_uses():
    def attention(layer):
        return [(layer, *i) for i in ITEMS if i[0] != "pv"]

    def norm(n):
        return [("x", n, cc) for cc in range(CC)]

    uses = norm(0) + [(n,) for n in ("c", "qc", "kc", "qr", "qs", "kr", "ks")] + [("v", 0, i) for i in range(2)]
    uses += attention(0) + [("o", 0, i) for i in range(2)]
    uses += norm(1) + [("router",)]
    for e in range(NEXP):
        uses += [("g", e), ("u", e)]
        if e:
            uses += [("d", e - 1, i) for i in range(2)]
    uses += [("d", NEXP - 1, i) for i in range(2)] + [("conv", i) for i in range(2)]
    uses += norm(2) + [("qk", hf, n) for hf in range(2) for n in range(2)] + [("v", 1, i) for i in range(2)]
    uses += attention(1) + [("o", 1, i) for i in range(2)]
    uses += norm(3) + [("f", n) for n in range(FT)]
    assert len(uses) % BANKS == 0, len(uses)
    return {u: n for n, u in enumerate(uses)}


USE = ring_uses()
ROUNDS = len(USE) // BANKS


class Signal:

    def __init__(self, sem, per_sequence, step=1, ahead=1):
        self.sem, self.per, self.step, self.ahead = sem, per_sequence, step, ahead

    def after(self, b, n):
        return (b * self.per + n + self.ahead) * self.step


def build(nc, x, wpack, wff, cpack, rpack, rope, piw_t, pv, oiw_t, op, out):
    with ExitStack() as top:
        def sem(name):
            return top.enter_context(nc.semaphore(name))

        def keep(name, shape, dt=F32):
            return top.enter_context(nc.sbuf_tensor(name, shape, dt))

        acts_sum = keep("acts_sum", [P, FT, B])
        ident = keep("ident", [P, P])
        build_layers(nc, top, sem, acts_sum, ident, x, wpack, wff, cpack, rpack, rope, out)
        build_patterns(nc, sem, acts_sum, ident, piw_t, pv, oiw_t, op, out)


def build_layers(nc, top, sem, acts_sum, ident, x, wpack, wff, cpack, rpack, rope, out):
    with ExitStack() as ctx:
        def sb(name, shape, dt=F32):
            return ctx.enter_context(nc.sbuf_tensor(name, shape, dt))

        wh = sb("wh", [P, W_COLS], F32R)
        wl = sb("wl", [P, W_COLS], F32R)
        wf = sb("wf", [P, CC, N_IN])
        cols = sb("cols", [P, C_COLS])
        rows = sb("rows", [P, R_COLS])
        cos_sin = sb("cos_sin", [P, 2, S])
        identb = sb("identb", [P, P], BF16)
        mask_q = sb("mask_q", [P, P], BF16)
        mask_k = sb("mask_k", [P, P], BF16)
        half_neg = sb("half_neg", [P, TT])
        q_stack = sb("q_stack", [STACK, 2, HH, S], F32R)
        k_stack = sb("k_stack", [STACK, 2, HH // 2, S], F32R)
        values = sb("values", [P, TT, H * VW + 32 - VW])

        scores_dram = nc.dram_tensor("scores_dram", [2, 4, P, S], F32, kind="Internal").ap()
        heads_dram = nc.dram_tensor("heads_dram", [2, 2, P, S], F32, kind="Internal").ap()
        recip_dram = nc.dram_tensor("recip_dram", [2, HH, S], F32, kind="Internal").ap()

        weights_loaded = sem("weights_loaded")
        consts_loaded = sem("consts_loaded")
        high_made = sem("high_made")
        low_made = sem("low_made")
        cleared = sem("cleared")
        cuts = [W_COLS * n // W_PARTS // 2 * 2 for n in range(W_PARTS)] + [W_COLS]
        widest = max(b - a for a, b in zip(cuts, cuts[1:]))

        with ExitStack() as tmp:
            staging = tmp.enter_context(nc.sbuf_tensor("staging", [P, widest], F32))
            block = tmp.enter_context(nc.Block())

            @block.sync
            def _(sp):
                sp.dma_start(staging[:, 0:cuts[1]], wpack[:, 0:cuts[1]]).then_inc(weights_loaded, SEM_DMA)
                sp.dma_start(wf[:, :, :], wff).then_inc(consts_loaded, SEM_DMA)
                sp.dma_start(cols[:, :], cpack).then_inc(consts_loaded, SEM_DMA)
                sp.dma_start(rows[:, :], rpack).then_inc(consts_loaded, SEM_DMA)
                sp.dma_start(cos_sin[:, :, :], rope).then_inc(consts_loaded, SEM_DMA)
                for n in range(1, W_PARTS):
                    sp.wait_ge(low_made, n)
                    sp.dma_start(staging[:, 0:cuts[n + 1] - cuts[n]], wpack[:, cuts[n]:cuts[n + 1]])\
                        .then_inc(weights_loaded, SEM_DMA)
                sp.wait_ge(consts_loaded, 4 * SEM_DMA)

            @block.vector
            def _(dve):
                for n in range(W_PARTS):
                    a, b = cuts[n], cuts[n + 1]
                    dve.wait_ge(weights_loaded, (n + 1) * SEM_DMA)
                    dve.tensor_copy(wh[:, a:b], staging[:, 0:b - a]).then_inc(high_made, 1)
                    dve.wait_ge(high_made, n + 1)
                    dve.tensor_tensor(wl[:, a:b], staging[:, 0:b - a], wh[:, a:b].bitcast(F32), ALU.subtract)\
                        .then_inc(low_made, 1)

            @block.gpsimd
            def _(pool):
                made = 0

                def step(ins):
                    nonlocal made
                    made += 1
                    ins.then_inc(cleared, 1)
                    pool.wait_ge(cleared, made)

                ones = values[:, :, 0:H * VW].rearrange("p t (h c) -> p t h c", c=VW)[:, :, :, HD:VW]
                for m, v in ((q_stack[:, :, :, :].bitcast(F32), 0.0), (k_stack[SHIFT:STACK, :, :, :].bitcast(F32), 1.0),
                             (half_neg[:, :], -0.5), (values[:, :, :], 0.0), (ones, 1.0), (ident[:, :], 0.0),
                             (identb[:, :], 0.0), (mask_q[:, :], 0.0), (mask_k[:, :], 0.0)):
                    step(nc.gpsimd.memset(m, v))
                for m in (ident, identb):
                    step(nc.gpsimd.affine_select(out=m[:, :], in_=m[:, :], compare_op=ALU.not_equal, fill=1.0,
                                                 base=0, pattern=[[-1, P]], channel_multiplier=1))
                for m, sign in ((mask_q, 1), (mask_k, -1)):
                    step(nc.gpsimd.affine_select(out=m[:, :], in_=m[:, :], compare_op=ALU.is_ge, fill=MASKED,
                                                 base=0, pattern=[[-sign, P]], channel_multiplier=sign))

        x_in = sb("x_in", [P, TT, E])
        xr = sb("xr", [P, TT, E])
        xh = sb("xh", [P, TT, E])
        xt_hi = sb("xt_hi", [P, CC, S], F32R)
        xt_lo = sb("xt_lo", [P, CC, S], F32R)
        full = sb("full", [P, 2, 2, S])
        xt_full, conv = full[:, 0, :, :], full[:, 1, :, :]
        qk = sb("qk", [P, 4, S], F32R)
        comp = sb("comp", [P, S])
        comp_hi = sb("comp_hi", [P, S], F32R)
        comp_lo = sb("comp_lo", [P, S], F32R)
        probs = sb("probs", [P, 2, 4, S])
        tanh_g, gate, hidden = probs[:, 0, 0:2, :], probs[:, 0, 2, :], probs[:, 0, 3, :]
        heads = sb("heads", [P, 2, S])
        relu_x = heads[:, :, :].rearrange("p g (t e) -> p (g t) e", e=E)
        dense = sb("dense", [P, S])
        recip_b = sb("recip_b", [P, S])
        tap_product = recip_b
        sums = sb("sums", [HH * 8, S // 8])
        recips = sb("recips", [HH * 8, S // 8])
        neg_max = sb("neg_max", [P, TT, HH])
        max_hi, max_lo = comp_hi[0:HH, :], comp_lo[0:HH, :]
        stats = sb("stats", [P, TT, 6])
        mean_var = sb("mean_var", [P, TT, 2])
        var_eps = sb("var_eps", [P, TT])
        rstd = sb("rstd", [P, TT])
        r_tanh = sb("r_tanh", [P, TT, NE])
        r_score = sb("r_score", [P, TT, NE])
        r_rank = sb("r_rank", [P, TT, NE])
        r_key = sb("r_key", [P, TT, NE])
        r_sel = sb("r_sel", [P, 2, TT, NE])
        r_top = sb("r_top", [P, 6, TT])
        cw = sb("cw", [P, TT, NE])
        cw_id = sb("cw_id", [P, TT])
        spare_pool = sb("spare_pool", [1, 1])
        spare_dve = sb("spare_dve", [1, 1])

        ring = ctx.enter_context(nc.psum_tensor("ring", [P, BANKS, S], F32))
        o_bank = ctx.enter_context(nc.psum_tensor("o_bank", [P, S], F32))

        bank_full = [sem(f"bank_full{n}") for n in range(BANKS)]

        signals = []

        def signal(name, per, step=1):
            signals.append(Signal(sem(name), per, step))
            return signals[-1]

        def pool_dma_signal(name, per):
            return Signal(sem(name), per, SEM_DMA, 0)

        bank_free = [signal(f"bank_free{n}", ROUNDS) for n in range(BANKS)]
        x_loaded = signal("x_loaded", 1, SEM_DMA)
        x_stored = signal("x_stored", 1, SEM_DMA)
        stats_made = signal("stats_made", 4)
        moments_made = signal("moments_made", 4)
        var_made = signal("var_made", 4)
        rstd_made = signal("rstd_made", 4)
        xh_made = signal("xh_made", 4)
        xt_hi_made = signal("xt_hi_made", 3 * CC)
        xt_full_made = signal("xt_full_made", CC)
        comp_hi_made = signal("comp_hi_made", 1)
        comp_lo_made = signal("comp_lo_made", 1)
        roped = signal("roped", 2)
        rope_gelu = signal("rope_gelu", 2)
        rope_term = signal("rope_term", 4)
        qk_hi_made = signal("qk_hi_made", 8)
        qk_lo_made = signal("qk_lo_made", 4)
        qk_stored = signal("qk_stored", 4, SEM_DMA)
        stacked = [signal(f"stacked{hf}", 24, SEM_DMA) for hf in range(2)]
        max_hi_made = signal("max_hi_made", 4)
        max_rows = [signal(f"max_rows{hf}", 4, SEM_DMA) for hf in range(2)]
        pv_done = signal("pv_done", 4 * 8)
        heads_made = signal("heads_made", 8)
        heads_stored = pool_dma_signal("heads_stored", 4)
        sums_loaded = pool_dma_signal("sums_loaded", 4)
        dense_loaded = pool_dma_signal("dense_loaded", 4)
        recip_made = signal("recip_made", 4)
        recip_stored = pool_dma_signal("recip_stored", 4)
        recip_spread = pool_dma_signal("recip_spread", 4)
        normed = signal("normed", 4)
        o_hi_made = signal("o_hi_made", 4)
        o_lo_made = signal("o_lo_made", 4)
        biased = signal("biased", 2)
        router = signal("router", 19)
        tanh_made = signal("tanh_made", NEXP)
        hidden_hi = signal("hidden_hi", NEXP)
        hidden_lo = signal("hidden_lo", NEXP)
        conv_step = signal("conv_step", 2 * TAPS * CC)
        id_added = signal("id_added", 1)
        relu_made = signal("relu_made", 1)
        halved = signal("halved", 1)
        relu_summed = signal("relu_summed", 1)
        pool_settled = signal("pool_settled", 4 * 5)

        first_step = sb("first_step", [1, len(signals)])

        def bank(use):
            return ring[:, USE[use] % BANKS, :]

        def wait_free(pe, b, use):
            u = USE[use]
            wait_for(pe, bank_free[u % BANKS], b, u // BANKS)

        def filled(use):
            return bank_full[USE[use] % BANKS]

        def freed(use):
            return bank_free[USE[use] % BANKS].sem

        def wait_full(eng, b, use):
            u = USE[use]
            eng.wait_ge(bank_full[u % BANKS], b * ROUNDS + u // BANKS + 1)

        def wait_read(eng, b, use):
            u = USE[use]
            wait_for(eng, bank_free[u % BANKS], b, u // BANKS + 1)

        def wait_for(eng, sig, b, n):
            eng.wait_ge(sig.sem, sig.after(b, n))

        def settle_pool(b):
            nonlocal settled
            wait_for(nc.gpsimd, pool_settled, b, settled)
            settled += 1
            nc.gpsimd.tensor_tensor(spare_pool[:, :], half_neg[0:1, 0:1], half_neg[0:1, 1:2], ALU.add)\
                .then_inc(pool_settled.sem, 1)

        def settle_dve():
            nc.vector.tensor_copy(spare_dve[:, :], half_neg[0:1, 0:1])

        settled = 0

        def span(causal, kt):
            return kt * P if causal else 0

        block = ctx.enter_context(nc.Block())

        @block.sync
        def _(sp):
            sp.dma_start(x_in[:, :, :], x[0].rearrange("(t p) e -> p t e", p=P)).then_inc(x_loaded.sem, SEM_DMA)
            with sp.Fori(0, B) as b:
                def stack(layer, hf):
                    n = 2 * layer + hf
                    if layer == 0:
                        wait_for(sp, qk_lo_made, b, 2 * hf + 2)
                    else:
                        for k in range(2):
                            wait_read(sp, b, ("qk", hf, k))
                    sp.wait_ge(stacked[hf].sem, stacked[hf].after(b, 12 * layer))
                    sp.dma_start(scores_dram[hf].rearrange("k p t -> p k t"), qk[:, :, :].bitcast(F32))\
                        .then_inc(qk_stored.sem, SEM_DMA)
                    wait_for(sp, qk_stored, b, n + 1)
                    parts = scores_dram[hf].rearrange("k (r p c) t -> k p c r t", p=2, c=HD)
                    for par in range(2):
                        for blk, (kq, kk) in enumerate(((0, 2), (0, 3), (1, 2))):
                            r0 = par * BLK + blk * HD
                            sp.dma_start(
                                q_stack[r0:r0 + HD, hf, :, :].rearrange("c (r p) t -> c p r t", p=2)[:, par]
                                .bitcast(F32), parts[kq, par]).then_inc(stacked[hf].sem, SEM_DMA)
                            sp.dma_start(k_stack[r0:r0 + HD, hf, :, :].bitcast(F32), parts[kk, par])\
                                .then_inc(stacked[hf].sem, SEM_DMA)

                def maxima(layer, hf):
                    wait_read(sp, b, (layer, "m", hf))
                    for n, part in enumerate((max_hi, max_lo)):
                        sp.dma_start(q_stack[SHIFT + n:SHIFT + n + 1, hf, :, :].bitcast(F32),
                                     part.bitcast(F32)).then_inc(max_rows[hf].sem, SEM_DMA)

                for layer in range(2):
                    stack(layer, 0)
                    stack(layer, 1)
                    maxima(layer, 0)
                    maxima(layer, 1)
                wait_read(sp, b, ("o", 1, 1))
                sp.dma_start(out[b].rearrange("(t p) e -> p t e", p=P), xr[:, :, :]).then_inc(x_stored.sem, SEM_DMA)
            wait_for(sp, x_loaded, B, 1)
            wait_for(sp, x_stored, B, 0)

        @block.gpsimd
        def _(pool):
            with pool.Fori(0, B) as b:
                def root(n):
                    wait_for(pool, var_made, b, n + 1)
                    nc.gpsimd.tensor_tensor(rstd[:, :], var_eps[:, :], half_neg[:, :], ALU.pow)\
                        .then_inc(rstd_made.sem, 1)

                def add_bias(tile, layer, at):
                    row = rows[:, at:at + E].unsqueeze(1).to_broadcast([P, TT, E])
                    nc.gpsimd.tensor_tensor(tile[:, :, :], tile[:, :, :], row, ALU.add).then_inc(biased.sem, 1)

                def normalise(layer, hf):
                    n = 2 * layer + hf
                    wait_for(pool, heads_made, b, 2 * n + 2)
                    settle_pool(b)
                    pool.dma_start(heads_dram[hf].rearrange("g p t -> p g t"), heads[:, :, :])\
                        .then_inc(heads_stored.sem, SEM_DMA)
                    wait_for(pool, heads_stored, b, n + 1)
                    settle_pool(b)
                    wait_for(pool, normed, b, n)
                    settle_pool(b)
                    by_head = heads_dram[hf].rearrange("g (j r) t -> (g j) r t", r=32)
                    pool.dma_start(sums[:, :], by_head[:, HD, :].rearrange("h (k i) -> h k i", k=8))\
                        .then_inc(sums_loaded.sem, SEM_DMA)
                    pool.dma_start(dense[:, :], by_head[:, 0:HD, :]).then_inc(dense_loaded.sem, SEM_DMA)
                    wait_for(pool, recip_made, b, n + 1)
                    settle_pool(b)
                    pool.dma_start(recip_dram[hf].rearrange("h (k i) -> h k i", k=8), recips[:, :])\
                        .then_inc(recip_stored.sem, SEM_DMA)
                    wait_for(pool, recip_stored, b, n + 1)
                    settle_pool(b)
                    pool.dma_start(recip_b[:, :], recip_dram[hf].unsqueeze(1).to_broadcast([HH, HD, S]))\
                        .then_inc(recip_spread.sem, SEM_DMA)

                root(0)
                wait_for(pool, xh_made, b, 1)
                add_bias(x_in, 0, R_BO0)
                normalise(0, 0)
                normalise(0, 1)
                root(1)
                steps = 0

                def conv_do(out_, in0, in1, how):
                    nonlocal steps
                    if steps:
                        wait_for(pool, conv_step, b, steps)
                    nc.gpsimd.tensor_tensor(out_, in0, in1, how).then_inc(conv_step.sem, 1)
                    steps += 1

                for cc in range(CC):
                    wait_for(pool, xt_full_made, b, cc + 1)
                    for s in range(TAPS):
                        w = C_CW + TAPS * cc + TAPS - 1 - s
                        tap = cols[:, w:w + 1].to_broadcast([P, S - s])
                        conv_do(tap_product[:, s:S] if s else conv[:, cc, :], xt_full[:, cc, 0:S - s], tap, ALU.mult)
                        more = tap_product[:, s:S] if s else cols[:, C_CB + cc:C_CB + cc + 1].to_broadcast([P, S])
                        conv_do(conv[:, cc, s:S], conv[:, cc, s:S], more, ALU.add)
                assert steps == conv_step.per
                root(2)
                wait_for(pool, xh_made, b, 3)
                add_bias(xr, 1, R_BO1)
                normalise(1, 0)
                normalise(1, 1)
                root(3)
                assert settled == pool_settled.per, settled

        @block.scalar
        def _(act):
            with act.Fori(0, B) as b:
                def copy_hi(n, cc, k):
                    wait_full(act, b, ("x", n, cc))
                    nc.scalar.activation(xt_hi[:, cc, :], bank(("x", n, cc)), ACT.Copy).then_inc(xt_hi_made.sem, 1)

                def copy_full(n, cc):
                    wait_full(act, b, ("x", n, cc))
                    return nc.scalar.activation(xt_full[:, cc, :], bank(("x", n, cc)), ACT.Copy)

                def attention(layer):
                    causal = layer == 0
                    units = 0
                    for kind, *i in ITEMS:
                        if kind == "m":
                            use = (layer, "m", i[0])
                            wait_full(act, b, use)
                            nc.scalar.activation(max_hi, bank(use)[0:HH, :], ACT.Copy)\
                                .then_inc(max_hi_made.sem, 1)
                        elif kind == "t":
                            hf, g, kt, j = i
                            use = (layer, "t", *i)
                            q0 = span(causal, kt)
                            n = (2 * layer + hf) * 8 + g * TT + kt
                            if j == 0 and n >= 2:
                                wait_for(act, pv_done, b, n - 1)
                            wait_full(act, b, use)
                            nc.scalar.activation(probs[:, n % 2, j, q0:S], bank(use)[:, q0:S], ACT.Exp, scale=SCALE)\
                                .then_inc(freed(use), 1)
                        elif kind == "pv" and i[2] == TT - 1:
                            hf, g, kt = i
                            n = 2 * (2 * layer + hf) + g
                            wait_for(act, pv_done, b, (2 * layer + hf) * 8 + g * TT + TT)
                            wait_for(act, recip_made, b, 2 * layer + hf)
                            nc.scalar.activation(heads[:, g, :], o_bank[:, :], ACT.Copy).then_inc(heads_made.sem, 1)

                for cc in range(CC):
                    copy_hi(0, cc, 0)
                for use, slot, bias in ((("c",), comp[:, :], C_BC), (("qc",), full[:, 0, 0, :], C_BQC),
                                        (("kc",), full[:, 0, 1, :], C_BKC)):
                    wait_full(act, b, use)
                    nc.scalar.activation(slot, bank(use), ACT.Gelu, bias=cols[:, bias:bias + 1]).then_inc(freed(use), 1)
                for k in range(2):
                    wait_for(act, roped, b, k + 1)
                    nc.scalar.activation(full[:, 1, k, :], full[:, 1, k, :], ACT.Gelu).then_inc(rope_gelu.sem, 1)
                attention(0)

                nxt = (b + 1) % B
                wait_read(act, b, ("o", 0, 1))
                act.dma_start(x_in[:, :, :], x[nxt].rearrange("(t p) e -> p t e", p=P))\
                    .then_inc(x_loaded.sem, SEM_DMA)
                for cc in range(CC):
                    copy_full(1, cc).then_inc(xt_full_made.sem, 1)
                    copy_hi(1, cc, 1)
                wait_full(act, b, ("router",))
                nc.scalar.activation(r_tanh[:, :, :].rearrange("p t e -> p (t e)"), bank(("router",))[:, 0:TT * NE],
                                     ACT.Tanh, scale=0.5).then_inc(freed(("router",)), 1)
                for e in range(NEXP):
                    if e >= 2:
                        wait_read(act, b, ("g", e - 2))
                    wait_full(act, b, ("g", e))
                    nc.scalar.activation(tanh_g[:, e % 2, :], bank(("g", e)), ACT.Tanh, scale=0.5)\
                        .then_inc(tanh_made.sem, 1)
                wait_for(act, router, b, 19)
                for t in range(TT):
                    last = nc.scalar.activation(relu_x[:, t, :], xh[:, t, :], ACT.Relu, scale=cw[:, t, NE - 1:NE])
                last.then_inc(relu_made.sem, 1)

                for cc in range(CC):
                    copy_hi(2, cc, 2)
                for hf in range(2):
                    for k in range(2):
                        use = ("qk", hf, k)
                        bias = (C_BQ1, C_BK1)[k] + hf
                        if k == 0:
                            wait_for(act, qk_stored, b, 2 + hf)
                        wait_full(act, b, use)
                        nc.scalar.activation(qk[:, 2 * k, :], bank(use), ACT.Identity, bias=cols[:, bias:bias + 1])\
                            .then_inc(qk_hi_made.sem, 1)
                attention(1)
                for cc in range(CC):
                    copy_full(3, cc).then_inc(freed(("x", 3, cc)), 1)
                for n in range(FT):
                    use = ("f", n)
                    wait_full(act, b, use)
                    nc.scalar.activation(bank(use), bank(use), ACT.Gelu,
                                         accum_out=acts_sum[:, n, bass.ds(b, 1)]).then_inc(freed(use), 1)

        @block.vector
        def _(dve):
            for n, s in enumerate(signals):
                nc.vector.memset(first_step[:, n:n + 1], 0.0).then_inc(s.sem, s.step)
            with dve.Fori(0, B) as b:
                def norm(n, src):
                    for t in range(TT):
                        last = nc.vector.bn_stats(stats[:, t, :], src[:, t, :])
                    last.then_inc(stats_made.sem, 1)
                    wait_for(dve, stats_made, b, n + 1)
                    settle_dve()
                    for t in range(TT):
                        last = nc.vector.bn_aggr(mean_var[:, t, :], stats[:, t, :])
                    last.then_inc(moments_made.sem, 1)
                    wait_for(dve, moments_made, b, n + 1)
                    nc.vector.tensor_scalar(var_eps[:, :], mean_var[:, :, 1], EPS, None, ALU.add)\
                        .then_inc(var_made.sem, 1)
                    wait_for(dve, rstd_made, b, n + 1)
                    for t in range(TT):
                        last = nc.vector.tensor_scalar(xh[:, t, :], src[:, t, :], mean_var[:, t, 0:1],
                                                       rstd[:, t:t + 1], ALU.subtract, ALU.mult)
                    last.then_inc(xh_made.sem, 1)

                def low_parts(n):
                    for cc in range(CC):
                        use = ("x", n, cc)
                        wait_for(dve, xt_hi_made, b, n * CC + cc + 1)
                        nc.vector.tensor_tensor(xt_lo[:, cc, :], bank(use), xt_hi[:, cc, :].bitcast(F32), ALU.subtract)\
                            .then_inc(freed(use), 1)

                def split_qk(hf, k):
                    n = 2 * hf + k
                    src = full[:, hf, k, :]
                    nc.vector.tensor_copy(qk[:, 2 * k, :], src).then_inc(qk_hi_made.sem, 1)
                    wait_for(dve, qk_hi_made, b, n + 1)
                    nc.vector.tensor_tensor(qk[:, 2 * k + 1, :], src, qk[:, 2 * k, :].bitcast(F32), ALU.subtract)\
                        .then_inc(qk_lo_made.sem, 1)

                def add_values(layer, bias):
                    out_v = values[:, :, 0:H * VW].rearrange("p t (h c) -> p t h c", c=VW)
                    row = rows[:, bias:bias + E].rearrange("p (h c) -> p h c", c=HD)
                    for i in range(2):
                        use = ("v", layer, i)
                        wait_full(dve, b, use)
                        for t in range(2):
                            src = bank(use)[:, t * E:(t + 1) * E].rearrange("p (h c) -> p h c", c=HD)
                            last = nc.vector.tensor_tensor(out_v[:, 2 * i + t, :, 0:HD], src, row, ALU.add)
                        last.then_inc(freed(use), 1)

                def normalise(layer, hf):
                    n = 2 * layer + hf
                    wait_for(dve, sums_loaded, b, n + 1)
                    nc.vector.reciprocal(recips[:, :], sums[:, :]).then_inc(recip_made.sem, 1)

                def scale_heads(layer, hf):
                    n = 2 * layer + hf
                    wait_for(dve, dense_loaded, b, n + 1)
                    wait_for(dve, recip_spread, b, n + 1)
                    nc.vector.tensor_tensor(comp[:, :], dense[:, :], recip_b[:, :], ALU.mult).then_inc(normed.sem, 1)
                    wait_for(dve, normed, b, n + 1)
                    nc.vector.tensor_copy(xt_hi[:, hf, :], comp[:, :]).then_inc(o_hi_made.sem, 1)
                    wait_for(dve, o_hi_made, b, n + 1)
                    nc.vector.tensor_tensor(xt_lo[:, hf, :], comp[:, :], xt_hi[:, hf, :].bitcast(F32), ALU.subtract)\
                        .then_inc(o_lo_made.sem, 1)

                def attention(layer):
                    causal = layer == 0
                    for kind, *i in ITEMS:
                        if kind == "s":
                            hf, hh, qt = i
                            use = (layer, "s", *i)
                            keys = (qt + 1) * P if causal else S
                            wait_full(dve, b, use)
                            nc.vector.tensor_reduce(neg_max[:, qt, hh:hh + 1], bank(use)[:, 0:keys], AX.X, ALU.max,
                                                    negate=True).then_inc(freed(use), 1)
                        elif kind == "m":
                            use = (layer, "m", i[0])
                            wait_for(dve, max_hi_made, b, 2 * layer + i[0] + 1)
                            nc.vector.tensor_tensor(max_lo, bank(use)[0:HH, :], max_hi.bitcast(F32),
                                                    ALU.subtract).then_inc(freed(use), 1)
                    for hf in range(2):
                        normalise(layer, hf)
                        scale_heads(layer, hf)

                def project_out(layer, src):
                    wait_for(dve, biased, b, layer + 1)
                    for i in range(2):
                        use = ("o", layer, i)
                        wait_full(dve, b, use)
                        nc.vector.tensor_tensor(xr[:, 2 * i:2 * i + 2, :], src[:, 2 * i:2 * i + 2, :],
                                                bank(use).rearrange("p (t e) -> p t e", e=E), ALU.add)\
                            .then_inc(freed(use), 1)

                wait_for(dve, x_loaded, b, 1)
                norm(0, x_in)
                low_parts(0)
                wait_read(dve, b, ("c",))
                nc.vector.tensor_copy(comp_hi[:, :], comp[:, :]).then_inc(comp_hi_made.sem, 1)
                wait_for(dve, comp_hi_made, b, 1)
                nc.vector.tensor_tensor(comp_lo[:, :], comp[:, :], comp_hi[:, :].bitcast(F32), ALU.subtract)\
                    .then_inc(comp_lo_made.sem, 1)
                for k, use in enumerate((("qc",), ("kc",))):
                    wait_read(dve, b, use)
                    split_qk(0, k)
                for k, (use, swapped, bias) in enumerate(((("qr",), ("qs",), C_BQR), (("kr",), ("ks",), C_BKR))):
                    wait_full(dve, b, use)
                    nc.vector.scalar_tensor_tensor(out=full[:, 1, k, :], in0=bank(use), scalar=cols[:, bias:bias + 1],
                                                   in1=cos_sin[:, 0, :], op0=ALU.add, op1=ALU.mult)\
                        .then_inc(freed(use), 1)
                    wait_full(dve, b, swapped)
                    if k:
                        wait_for(dve, roped, b, k)
                    else:
                        wait_for(dve, comp_lo_made, b, 1)
                    nc.vector.scalar_tensor_tensor(out=comp[:, :], in0=bank(swapped),
                                                   scalar=cols[:, bias + 1:bias + 2], in1=cos_sin[:, 1, :],
                                                   op0=ALU.add, op1=ALU.mult).then_inc(freed(swapped), 1)
                    wait_read(dve, b, use)
                    wait_read(dve, b, swapped)
                    nc.vector.tensor_tensor(full[:, 1, k, :], full[:, 1, k, :], comp[:, :], ALU.add)\
                        .then_inc(roped.sem, 1)
                add_values(0, R_BV0)
                wait_for(dve, qk_stored, b, 1)
                for k in range(2):
                    wait_for(dve, rope_gelu, b, k + 1)
                    split_qk(1, k)
                attention(0)
                wait_for(dve, x_stored, b, 0)
                project_out(0, x_in)

                wait_read(dve, b, ("o", 0, 1))
                norm(1, xr)
                low_parts(1)
                steps = 0

                def step(ins):
                    nonlocal steps
                    steps += 1
                    ins.then_inc(router.sem, 1)
                    wait_for(dve, router, b, steps)

                wait_read(dve, b, ("router",))
                bias = rows[:, R_BR:R_BR + TT * NE].rearrange("p (t e) -> p t e", e=NE)
                rev = rows[:, R_REV:R_REV + TT * NE].rearrange("p (t e) -> p t e", e=NE)

                def every(col):
                    return col.unsqueeze(2).to_broadcast([P, TT, NE])

                step(nc.vector.tensor_scalar(r_score[:, :, :], r_tanh[:, :, :], 0.5, 0.5, ALU.mult, ALU.add))
                step(nc.vector.tensor_tensor(r_rank[:, :, :], r_score[:, :, :], bias, ALU.add))
                for k in range(2):
                    top_v, top_k = r_top[:, 2 * k, :], r_top[:, 2 * k + 1, :]
                    step(nc.vector.tensor_reduce(top_v, r_rank[:, :, :], AX.X, ALU.max))
                    step(nc.vector.tensor_tensor(r_key[:, :, :], r_rank[:, :, :], every(top_v), ALU.is_equal))
                    step(nc.vector.tensor_tensor(r_key[:, :, :], r_key[:, :, :], rev, ALU.mult))
                    step(nc.vector.tensor_reduce(top_k, r_key[:, :, :], AX.X, ALU.max))
                    step(nc.vector.tensor_tensor(r_sel[:, k, :, :], r_key[:, :, :], every(top_k), ALU.is_equal))
                    if k == 0:
                        step(nc.vector.scalar_tensor_tensor(out=r_rank[:, :, :], in0=r_sel[:, 0, :, :], scalar=LOWEST,
                                                            in1=r_rank[:, :, :], op0=ALU.mult, op1=ALU.add))
                step(nc.vector.tensor_tensor(r_key[:, :, :], r_sel[:, 0, :, :], r_sel[:, 1, :, :], ALU.add))
                step(nc.vector.tensor_tensor(r_key[:, :, :], r_key[:, :, :], r_score[:, :, :], ALU.mult))
                step(nc.vector.tensor_reduce(r_top[:, 4, :], r_key[:, :, :], AX.X, ALU.add))
                step(nc.vector.tensor_scalar(r_top[:, 4, :], r_top[:, 4, :], 1e-9, None, ALU.add))
                step(nc.vector.reciprocal(r_top[:, 5, :], r_top[:, 4, :]))
                step(nc.vector.tensor_tensor(cw[:, :, :], r_key[:, :, :], every(r_top[:, 5, :]), ALU.mult))
                assert steps == router.per, steps
                nc.vector.tensor_tensor(cw_id[:, :], cw[:, :, NEXP], cw[:, :, NEXP + 2], ALU.add)\
                    .then_inc(id_added.sem, 1)
                wait_for(dve, id_added, b, 1)
                for t in range(TT):
                    last = nc.vector.scalar_tensor_tensor(out=xr[:, t, :], in0=xh[:, t, :], scalar=cw_id[:, t:t + 1],
                                                          in1=xr[:, t, :], op0=ALU.mult, op1=ALU.add)
                nc.vector.tensor_scalar(cw[:, :, 0:NEXP], cw[:, :, 0:NEXP], 0.5, None, ALU.mult)\
                    .then_inc(halved.sem, 1)
                wait_for(dve, halved, b, 1)

                def add_expert(e):
                    for i in range(2):
                        use = ("d", e, i)
                        if e:
                            wait_read(dve, b, ("d", e - 1, i))
                        wait_full(dve, b, use)
                        for t in range(2):
                            tt = 2 * i + t
                            last = nc.vector.scalar_tensor_tensor(
                                out=xr[:, tt, :], in0=bank(use)[:, t * E:(t + 1) * E], scalar=cw[:, tt, e:e + 1],
                                in1=xr[:, tt, :], op0=ALU.mult, op1=ALU.add)
                        last.then_inc(freed(use), 1)

                for e in range(NEXP):
                    wait_for(dve, tanh_made, b, e + 1)
                    nc.vector.scalar_tensor_tensor(out=gate, in0=tanh_g[:, e % 2, :], scalar=1.0, in1=bank(("g", e)),
                                                   op0=ALU.add, op1=ALU.mult).then_inc(freed(("g", e)), 1)
                    wait_full(dve, b, ("u", e))
                    wait_read(dve, b, ("g", e))
                    if e:
                        wait_for(dve, hidden_lo, b, e)
                    nc.vector.tensor_tensor(hidden, gate, bank(("u", e)), ALU.mult).then_inc(freed(("u", e)), 1)
                    wait_read(dve, b, ("u", e))
                    if e >= 2:
                        wait_full(dve, b, ("d", e - 2, 1))
                    nc.vector.tensor_copy(qk[:, 2 * (e % 2), :], hidden).then_inc(hidden_hi.sem, 1)
                    wait_for(dve, hidden_hi, b, e + 1)
                    nc.vector.tensor_tensor(qk[:, 2 * (e % 2) + 1, :], hidden, qk[:, 2 * (e % 2), :].bitcast(F32),
                                            ALU.subtract).then_inc(hidden_lo.sem, 1)
                    if e:
                        add_expert(e - 1)
                add_expert(NEXP - 1)
                for i in range(2):
                    use = ("conv", i)
                    wait_read(dve, b, ("d", NEXP - 1, i))
                    wait_full(dve, b, use)
                    part = xr[:, 2 * i:2 * i + 2, :]
                    nc.vector.tensor_tensor(part, part, bank(use).rearrange("p (t e) -> p t e", e=E), ALU.add)\
                        .then_inc(freed(use), 1)
                wait_for(dve, relu_made, b, 1)
                wait_read(dve, b, ("conv", 1))
                nc.vector.tensor_tensor(xr[:, :, :], xr[:, :, :], relu_x, ALU.add)\
                    .then_inc(relu_summed.sem, 1)
                wait_for(dve, relu_summed, b, 1)

                norm(2, xr)
                low_parts(2)
                for hf in range(2):
                    for k in range(2):
                        use = ("qk", hf, k)
                        bias = (C_BQ1, C_BK1)[k] + hf
                        wait_for(dve, qk_hi_made, b, 4 + 2 * hf + k + 1)
                        nc.vector.scalar_tensor_tensor(out=qk[:, 2 * k + 1, :], in0=bank(use),
                                                       scalar=cols[:, bias:bias + 1], in1=qk[:, 2 * k, :].bitcast(F32),
                                                       op0=ALU.add, op1=ALU.subtract).then_inc(freed(use), 1)
                add_values(1, R_BV1)
                attention(1)
                project_out(1, xr)

                wait_read(dve, b, ("o", 1, 1))
                norm(3, xr)
                wait_full(dve, b, ("x", 3, CC - 1))

        @block.tensor
        def _(pe):
            with pe.Fori(0, B) as b:
                def turn(n):
                    wait_for(pe, xh_made, b, n + 1)
                    for cc in range(CC):
                        use = ("x", n, cc)
                        wait_free(pe, b, use)
                        for t in range(TT):
                            last = nc.tensor.transpose(bank(use)[:, t * P:(t + 1) * P],
                                                       xh[:, t, cc * P:(cc + 1) * P], ident[:, :])
                        last.then_inc(filled(use), 1)

                def product(dst, lhs, rhs):
                    terms = [(l[i], r[k]) for l, r in zip(lhs, rhs) for i, k in ((0, 0), (0, 1), (1, 0))]
                    for n, (l, r) in enumerate(terms):
                        last = nc.tensor.matmul(dst, l, r, start=n == 0, stop=n == len(terms) - 1)
                    return last

                def weight(at, n):
                    return wh[:, at:at + n], wl[:, at:at + n]

                def xt(cc, t=None):
                    s = slice(0, S) if t is None else slice(t * P, (t + 1) * P)
                    return xt_hi[:, cc, s], xt_lo[:, cc, s]

                def channels(use, at, width=P):
                    wait_free(pe, b, use)
                    product(bank(use), [weight(at + cc * width, P) for cc in range(CC)],
                            [xt(cc) for cc in range(CC)]).then_inc(filled(use), 1)

                def tokens(use, i, ats):
                    wait_free(pe, b, use)
                    for t in range(2):
                        last = product(bank(use)[:, t * E:(t + 1) * E], [xt(cc, 2 * i + t) for cc in range(CC)],
                                       [weight(at, E) for at in ats])
                    last.then_inc(filled(use), 1)

                def scores(layer, hf, hh, qt):
                    causal = layer == 0
                    use = (layer, "s", hf, hh, qt)
                    keys = (qt + 1) * P if causal else S
                    wait_free(pe, b, use)
                    last = nc.tensor.matmul(bank(use)[:, 0:keys], q_stack[0:SHIFT, hf, hh, qt * P:(qt + 1) * P],
                                            k_stack[0:SHIFT, hf, hh // 2, 0:keys], start=True, stop=not causal)
                    if causal:
                        last = nc.tensor.matmul(bank(use)[:, qt * P:keys], identb[:, :], mask_q[:, :],
                                                start=False, stop=True)
                    last.then_inc(filled(use), 1)

                def scores_t(layer, hf, g, kt, j):
                    causal = layer == 0
                    use = (layer, "t", hf, g, kt, j)
                    hh = 4 * g + j
                    q0 = span(causal, kt)
                    wait_free(pe, b, use)
                    last = nc.tensor.matmul(bank(use)[:, q0:S], k_stack[:, hf, hh // 2, kt * P:(kt + 1) * P],
                                            q_stack[:, hf, hh, q0:S], start=True, stop=not causal)
                    if causal:
                        last = nc.tensor.matmul(bank(use)[:, q0:q0 + P], identb[:, :], mask_k[:, :],
                                                start=False, stop=True)
                    last.then_inc(filled(use), 1)

                def weigh(layer, hf, g, kt):
                    q0 = span(layer == 0, kt)
                    n = (2 * layer + hf) * 8 + g * TT + kt
                    wait_read(pe, b, (layer, "t", hf, g, kt, 3))
                    if kt == 0:
                        wait_for(pe, heads_made, b, 2 * (2 * layer + hf) + g)
                    for j in range(4):
                        h = HH * hf + 4 * g + j
                        last = nc.tensor.matmul(o_bank[32 * j:32 * j + 32, q0:S], values[:, kt, h * VW:h * VW + 32],
                                                probs[:, n % 2, j, q0:S], start=kt == 0, stop=kt == TT - 1,
                                                skip_group_check=True)
                    last.then_inc(pv_done.sem, 1)

                def attention(layer):
                    wait_for(pe, stacked[0], b, 12 * (layer + 1))
                    started = False
                    for kind, *i in ITEMS:
                        if kind == "s":
                            if i[0] == 1 and not started:
                                wait_for(pe, stacked[1], b, 12 * (layer + 1))
                                started = True
                            scores(layer, *i)
                        elif kind == "m":
                            use = (layer, "m", i[0])
                            wait_free(pe, b, use)
                            wait_read(pe, b, (layer, "s", i[0], HH - 1, TT - 1))
                            for t in range(TT):
                                last = nc.tensor.transpose(bank(use)[0:HH, t * P:(t + 1) * P], neg_max[:, t, :],
                                                           ident[:, :])
                            last.then_inc(filled(use), 1)
                        elif kind == "t":
                            if i[1:] == [0, 0, 0]:
                                wait_for(pe, max_rows[i[0]], b, 2 * (layer + 1))
                            scores_t(layer, *i)
                        else:
                            weigh(layer, *i)

                def project_out(layer, at):
                    wait_for(pe, o_lo_made, b, 2 * layer + 2)
                    for i in range(2):
                        tokens(("o", layer, i), i, [at + cc * E for cc in range(CC)])

                turn(0)
                wait_read(pe, b, ("x", 0, 1))
                channels(("c",), W_C)
                wait_for(pe, comp_lo_made, b, 1)
                for use, at in ((("qc",), W_QC), (("kc",), W_KC)):
                    wait_free(pe, b, use)
                    product(bank(use), [weight(at, P)], [(comp_hi[:, :], comp_lo[:, :])]).then_inc(filled(use), 1)
                for use, at in ((("qr",), W_QR), (("qs",), W_QS), (("kr",), W_KR), (("ks",), W_KS)):
                    channels(use, at)
                for i in range(2):
                    use = ("v", 0, i)
                    wait_free(pe, b, use)
                    for t in range(2):
                        s = slice((2 * i + t) * P, (2 * i + t + 1) * P)
                        last = product(bank(use)[:, t * E:(t + 1) * E], [(comp_hi[:, s], comp_lo[:, s])],
                                       [weight(W_V0, E)])
                    last.then_inc(filled(use), 1)
                attention(0)
                project_out(0, W_O0)

                turn(1)
                wait_read(pe, b, ("x", 1, 1))
                use = ("router",)
                wait_free(pe, b, use)
                for t in range(TT):
                    last = product(bank(use)[:, t * NE:(t + 1) * NE], [xt(cc, t) for cc in range(CC)],
                                   [weight(W_R + cc * NE, NE) for cc in range(CC)])
                last.then_inc(filled(use), 1)

                def expert_down(e):
                    wait_for(pe, hidden_lo, b, e + 1)
                    for i in range(2):
                        use = ("d", e, i)
                        wait_free(pe, b, use)
                        for t in range(2):
                            s = slice((2 * i + t) * P, (2 * i + t + 1) * P)
                            last = product(bank(use)[:, t * E:(t + 1) * E],
                                           [(qk[:, 2 * (e % 2), s], qk[:, 2 * (e % 2) + 1, s])],
                                           [weight(W_D + e * E, E)])
                        last.then_inc(filled(use), 1)

                for e in range(NEXP):
                    for k, name in enumerate("gu"):
                        channels((name, e), W_GU + (2 * e + k) * INNER, NEXP * 2 * INNER)
                    if e:
                        expert_down(e - 1)
                expert_down(NEXP - 1)
                wait_for(pe, conv_step, b, 2 * TAPS * CC)
                for i in range(2):
                    use = ("conv", i)
                    wait_free(pe, b, use)
                    for t in range(2):
                        for cc in range(CC):
                            at = t * E + cc * P
                            last = nc.tensor.transpose(bank(use)[:, at:at + P],
                                                       conv[:, cc, (2 * i + t) * P:(2 * i + t + 1) * P], ident[:, :])
                    last.then_inc(filled(use), 1)

                turn(2)
                wait_read(pe, b, ("x", 2, 1))
                for hf in range(2):
                    for k in range(2):
                        channels(("qk", hf, k), W_QK1 + k * E + hf * P, 2 * E)
                for i in range(2):
                    tokens(("v", 1, i), i, [W_V1 + cc * E for cc in range(CC)])
                attention(1)
                project_out(1, W_O1)

                turn(3)
                wait_read(pe, b, ("x", 3, 1))
                for n in range(FT):
                    use = ("f", n)
                    wait_free(pe, b, use)
                    for cc in range(CC):
                        last = nc.tensor.matmul(bank(use), wf[:, cc, n * P:(n + 1) * P], xt_full[:, cc, :],
                                                start=cc == 0, stop=cc == CC - 1)
                    last.then_inc(filled(use), 1)


def build_patterns(nc, sem, acts_sum, ident, piw_t, pv, oiw_t, op, out):
    NP, NO = N_PROC // P, N_OUT // P
    RING = 4
    TILES = min(8, B)
    with ExitStack() as ctx:
        def sb(name, shape, dt=F32):
            return ctx.enter_context(nc.sbuf_tensor(name, shape, dt))

        piw = sb("piw", [P, RING, N_PROC])
        pvs = sb("pvs", [P, NP, D_PV])
        oiw = sb("oiw", [P, N_OUT])
        ops = sb("ops", [P, NO, E])
        acts = sb("acts", [B, N_IN])
        work = sb("work", [B, N_IN])
        chosen = sb("chosen", [B, N_IN])
        turned = sb("turned", [P, FT, B])
        top8 = sb("top8", [B, 8])
        small = sb("small", [B, 4])
        agg = sb("agg", [P, B])
        outp = sb("outp", [B, E])
        pick = sb("pick", [B, B, P])
        tiles = sb("tiles", [P, TILES, TT, E])
        ps = ctx.enter_context(nc.psum_tensor("ps", [P, 8, S], F32))

        loaded = sem("tail_loaded")
        piw_loaded = [sem(f"piw_loaded{n}") for n in range(RING)]
        piw_used = sem("piw_used")
        pick_made = sem("pick_made")
        turned_in = sem("turned_in")
        t_step = sem("tail_step")
        p_step = sem("tail_matmuls")
        a_step = sem("tail_activations")
        tile_loaded = [sem(f"tile_loaded{n}") for n in range(TILES)]
        tile_summed = sem("tile_summed")
        spread = sem("spread")
        tile_stored = [sem(f"tile_stored{n}") for n in range(TILES)]

        def tile_of(b):
            return out[b].rearrange("(t p) e -> p t e", p=P)

        block = ctx.enter_context(nc.Block())
        marks = []
        P_ACTS, P_TURN_IN, P_PROC, P_TURN_PROC, P_AGG, P_OUT, P_TURN_OUT, P_OUTP = range(1, 9)

        @block.sync
        def _(sp):
            for n in range(RING):
                sp.dma_start(piw[:, n, :], piw_t[n * P:(n + 1) * P, :]).then_inc(piw_loaded[n], SEM_DMA)
            sp.dma_start(pvs[:, :, :], pv.rearrange("(n p) d -> p n d", p=P)).then_inc(loaded, SEM_DMA)
            sp.dma_start(oiw[:, :], oiw_t).then_inc(loaded, SEM_DMA)
            sp.dma_start(ops[:, :, :], op.rearrange("(n p) e -> p n e", p=P)).then_inc(loaded, SEM_DMA)
            for b in range(TILES):
                sp.dma_start(tiles[:, b, :, :], tile_of(b)).then_inc(tile_loaded[b], SEM_DMA)
            for n in range(RING, FT):
                sp.wait_ge(piw_used, n - RING + 1)
                sp.dma_start(piw[:, n % RING, :], piw_t[n * P:(n + 1) * P, :]).then_inc(piw_loaded[n % RING], SEM_DMA)
            for b in range(B):
                sp.wait_ge(tile_summed, b + 1)
                sp.dma_start(tile_of(b), tiles[:, b % TILES, :, :]).then_inc(tile_stored[b % TILES], SEM_DMA)
                if b + TILES // 2 >= TILES and b + TILES // 2 < B:
                    n = b + TILES // 2
                    sp.wait_ge(tile_stored[n % TILES], SEM_DMA * (n // TILES))
                    sp.dma_start(tiles[:, n % TILES, :, :], tile_of(n)).then_inc(tile_loaded[n % TILES], SEM_DMA)
            for n in range(TILES):
                sp.wait_ge(tile_stored[n], SEM_DMA * (B // TILES))

        @block.gpsimd
        def _(pool):
            nc.gpsimd.memset(pick[:, :, :], 0.0).then_inc(pick_made, 1)
            pool.wait_ge(pick_made, 1)
            nc.gpsimd.affine_select(out=pick[:, :, :], in_=pick[:, :, :], compare_op=ALU.not_equal, fill=1.0,
                                    base=0, pattern=[[-1, B], [0, P]], channel_multiplier=1).then_inc(pick_made, 1)

        @block.vector
        def _(dve):
            done = 0


            def step(ins):
                nonlocal done
                done += 1
                ins.then_inc(t_step, 1)
                dve.wait_ge(t_step, done)

            def take_out(width, k):
                for n in range(k // 8):
                    src = acts if n == 0 else work
                    step(nc.vector.max(top8[:, :], src[:, 0:width]))
                    if n == 0:
                        step(nc.vector.tensor_copy(small[:, 0:1], top8[:, 0:1]))
                    step(nc.vector.match_replace(out=work[:, 0:width], in_to_replace=top8[:, :],
                                                 in_values=src[:, 0:width], imm_value=LOWEST))

            def choose(width, k):
                take_out(width, k)
                step(nc.vector.tensor_tensor(work[:, 0:width], work[:, 0:width], acts[:, 0:width], ALU.not_equal))
                step(nc.vector.tensor_tensor(chosen[:, 0:width], work[:, 0:width], acts[:, 0:width], ALU.mult))

            dve.wait_ge(p_step, P_ACTS)
            step(nc.vector.tensor_scalar(acts[:, :], ps[0:B, 0:4, :].rearrange("p n t -> p (n t)"), 1.0 / S, None,
                                         ALU.mult))
            choose(N_IN, K_IN)  
            marks.append(done)
            dve.wait_ge(p_step, P_TURN_IN)
            step(nc.vector.tensor_copy(turned[:, :, :].rearrange("p n b -> p (n b)"), ps[:, 4, 0:FT * B]))
            marks.append(done)
            dve.wait_ge(a_step, 1)
            take_out(N_PROC, K_PROC)
            step(nc.vector.tensor_tensor(work[:, 0:N_PROC], work[:, 0:N_PROC], acts[:, 0:N_PROC], ALU.not_equal))
            step(nc.vector.tensor_scalar(small[:, 1:2], small[:, 0:1], -1.0, None, ALU.mult))
            marks.append(done)
            dve.wait_ge(a_step, 2)
            step(nc.vector.tensor_tensor(chosen[:, 0:N_PROC], chosen[:, 0:N_PROC], work[:, 0:N_PROC], ALU.mult))
            step(nc.vector.tensor_reduce(small[:, 2:3], chosen[:, 0:N_PROC], AX.X, ALU.add))
            step(nc.vector.reciprocal(small[:, 3:4], small[:, 2:3]))
            step(nc.vector.tensor_scalar(chosen[:, 0:N_PROC], chosen[:, 0:N_PROC], small[:, 3:4], None, ALU.mult))
            marks.append(done)
            dve.wait_ge(p_step, P_TURN_PROC)
            step(nc.vector.tensor_copy(turned[:, 0:NP, :].rearrange("p n b -> p (n b)"), ps[:, 4, 0:NP * B]))
            marks.append(done)
            dve.wait_ge(p_step, P_AGG)
            step(nc.vector.tensor_copy(agg[:, :], ps[:, 5, 0:B]))
            marks.append(done)
            dve.wait_ge(a_step, 3)
            choose(N_OUT, K_OUT)
            marks.append(done)
            dve.wait_ge(p_step, P_TURN_OUT)
            step(nc.vector.tensor_copy(turned[:, :, :].rearrange("p n b -> p (n b)"), ps[:, 4, 0:NO * B]))
            marks.append(done)
            dve.wait_ge(p_step, P_OUTP)
            step(nc.vector.tensor_copy(outp[:, :], ps[0:B, 5, 0:E]))
            marks.append(done)
            for b in range(B):
                dve.wait_ge(spread, b + 1)
                dve.wait_ge(tile_loaded[b % TILES], SEM_DMA * (b // TILES + 1))
                row = ps[:, b % 4, 0:E].unsqueeze(1).to_broadcast([P, TT, E])
                nc.vector.tensor_tensor(tiles[:, b % TILES, :, :], tiles[:, b % TILES, :, :], row, ALU.add)\
                    .then_inc(tile_summed, 1)

        (IN_CHOSEN, IN_TURNED, PROC_TAKEN, PROC_WEIGHTS, PROC_TURNED, AGG_MADE, OUT_CHOSEN, OUT_TURNED,
         OUTP_MADE) = marks

        @block.scalar
        def _(act):
            act.wait_ge(p_step, P_PROC)
            act.wait_ge(t_step, IN_TURNED)
            nc.scalar.activation(acts[:, 0:N_PROC], ps[0:B, 0:2, :].rearrange("p n t -> p (n t)"), ACT.Gelu)\
                .then_inc(a_step, 1)
            act.wait_ge(t_step, PROC_TAKEN)
            nc.scalar.activation(chosen[:, 0:N_PROC], acts[:, 0:N_PROC], ACT.Exp, bias=small[:, 1:2])\
                .then_inc(a_step, 1)
            act.wait_ge(p_step, P_OUT)
            nc.scalar.activation(acts[:, :], ps[0:B, 0:4, :].rearrange("p n t -> p (n t)"), ACT.Gelu)\
                .then_inc(a_step, 1)

        @block.tensor
        def _(pe):
            def turn_back(n):
                for k in range(n):
                    last = nc.tensor.transpose(ps[:, 4, k * B:(k + 1) * B], chosen[:, k * P:(k + 1) * P],
                                               ident[0:B, 0:B])
                last.then_inc(p_step, 1)

            for n in range(FT):
                last = nc.tensor.transpose(ps[0:B, n // 4, n % 4 * P:(n % 4 + 1) * P], acts_sum[:, n, :], ident[:, :])
            last.then_inc(p_step, 1)
            pe.wait_ge(t_step, IN_CHOSEN)
            turn_back(FT)
            pe.wait_ge(t_step, IN_TURNED)
            for n in range(FT):
                pe.wait_ge(piw_loaded[n % RING], SEM_DMA * (n // RING + 1))
                for half in range(2):
                    last = nc.tensor.matmul(ps[0:B, half, :], turned[:, n, :], piw[:, n % RING, half * S:(half + 1) * S],
                                            start=n == 0, stop=n == FT - 1)
                last.then_inc(piw_used, 1)
            pe.wait_ge(piw_used, FT)
            nc.tensor.transpose(ps[:, 7, 0:B], ident[0:B, :], ident[0:B, 0:B]).then_inc(p_step, 1)
            pe.wait_ge(loaded, 3 * SEM_DMA)
            pe.wait_ge(t_step, PROC_WEIGHTS)
            turn_back(NP)
            pe.wait_ge(t_step, PROC_TURNED)
            for n in range(NP):
                last = nc.tensor.matmul(ps[:, 5, 0:B], pvs[:, n, :], turned[:, n, :], start=n == 0, stop=n == NP - 1)
            last.then_inc(p_step, 1)
            pe.wait_ge(t_step, AGG_MADE)
            for n in range(4):
                last = nc.tensor.matmul(ps[0:B, n, :], agg[:, :], oiw[:, n * S:(n + 1) * S], start=True, stop=True)
            last.then_inc(p_step, 1)
            pe.wait_ge(t_step, OUT_CHOSEN)
            turn_back(NO)
            pe.wait_ge(t_step, OUT_TURNED)
            for n in range(NO):
                last = nc.tensor.matmul(ps[0:B, 5, 0:E], turned[:, n, :], ops[:, n, :], start=n == 0, stop=n == NO - 1)
            last.then_inc(p_step, 1)
            pe.wait_ge(t_step, OUTP_MADE)
            pe.wait_ge(pick_made, 2)
            for b in range(B):
                if b >= 4:
                    pe.wait_ge(tile_summed, b - 3)
                nc.tensor.matmul(ps[:, b % 4, 0:E], pick[:, b, :], outp[:, :], start=True, stop=True)\
                    .then_inc(spread, 1)


def _by_partition(w):
    k, n = w.shape
    return w.reshape(k // P, P, n).transpose(1, 0, 2).reshape(P, -1)


def _layout(i):
    f = np.float32
    g = {k: np.asarray(v) for k, v in i.items()}
    zeros = np.zeros((64, 1), f)

    def swapped(w):
        return np.concatenate([w[..., 64:], w[..., :64]], -1)

    def low(w):
        return np.concatenate([w, np.broadcast_to(zeros, (64, w.shape[1]))], 0)

    def high(w):
        return np.concatenate([np.broadcast_to(zeros, (64, w.shape[1])), w], 0)

    wgu = np.stack([g["L0_ffn_Wg"], g["L0_ffn_Wu"]], 1)
    wgu = wgu.transpose(2, 0, 1, 3).reshape(E, NEXP * 2 * INNER)
    wqkv = g["L1_attn_Wqkv"]
    parts = [
        _by_partition(np.concatenate([g["L0_attn_wq"], g["L0_attn_wkv"]], 1)),
        _by_partition(g["L0_attn_wqr"]), _by_partition(swapped(g["L0_attn_wqr"])),
        _by_partition(g["L0_attn_wkr"]), _by_partition(swapped(g["L0_attn_wkr"])),
        low(g["L0_attn_wqc"]), high(g["L0_attn_wkc"]), high(g["L0_attn_wv"]),
        _by_partition(g["L0_attn_wo"]), _by_partition(wqkv[:, :2 * E]), _by_partition(wqkv[:, 2 * E:]),
        _by_partition(g["L1_attn_Wo"]), _by_partition(wgu),
        g["L0_ffn_Wd"].transpose(1, 0, 2).reshape(INNER, NEXP * E), _by_partition(g["L0_ffn_Wr"]),
    ]
    wpack = np.ascontiguousarray(np.concatenate(parts, 1))
    assert wpack.shape == (P, W_COLS)
    wff = np.ascontiguousarray(g["L1_ffn_input_patterns"].T.reshape(CC, P, N_IN).transpose(1, 0, 2))
    bqkv = g["L1_attn_bqkv"]
    conv_w = g["L0_ffn_conv_w"].reshape(TAPS, CC, P)
    columns = [np.concatenate([g["L0_attn_bq"], g["L0_attn_bkv"]]), g["L0_attn_bqc"], g["L0_attn_bkc"],
               g["L0_attn_bqr"], swapped(g["L0_attn_bqr"]), g["L0_attn_bkr"], swapped(g["L0_attn_bkr"])]
    columns += [bqkv[n * P:(n + 1) * P] for n in range(4)]
    columns += [conv_w[k, cc] for cc in range(CC) for k in range(TAPS)]
    columns += [g["L0_ffn_conv_b"][cc * P:(cc + 1) * P] for cc in range(CC)]
    cpack = np.ascontiguousarray(np.stack(columns, 1))
    rev = np.arange(NE, 0, -1).astype(f)
    row = np.concatenate([g["L0_attn_bv"], g["L0_attn_bo"], bqkv[2 * E:], g["L1_attn_bo"],
                          *[g["L0_ffn_router_bias"]] * TT, *[rev] * TT])
    rpack = np.ascontiguousarray(np.broadcast_to(row, (P, R_COLS)))
    inv = (f(1.0) / (f(10000.0) ** (np.arange(0, P, 2).astype(f) / f(P)))).astype(f)
    angle = (np.arange(S).astype(f)[:, None] * inv[None, :]).astype(f)
    angle = np.concatenate([angle, angle], 1).T
    sign = np.where(np.arange(P) < P // 2, f(-1), f(1))[:, None]
    rope = np.ascontiguousarray(np.stack([np.cos(angle), np.sin(angle) * sign], 1).astype(f))
    return dict(x=np.ascontiguousarray(g["L0_attn_x"]), wpack=wpack, wff=wff, cpack=cpack, rpack=rpack, rope=rope,
                piw_t=np.ascontiguousarray(g["L1_ffn_process_input_weights"].T), pv=g["L1_ffn_process_values"],
                oiw_t=np.ascontiguousarray(g["L1_ffn_output_input_weights"].T), op=g["L1_ffn_output_patterns"])


def kernel(**inputs):
    import concourse.bacc as _bacc
    from concourse.bass_utils import run_bass_kernel_spmd as _run

    nc = _bacc.Bacc("TRN2", target_bir_lowering=False, num_devices=1)
    arrays, args = {}, {}
    for name, a in _layout(inputs).items():
        arrays[f"in_{name}"] = a
        args[name] = nc.dram_tensor(f"in_{name}", a.shape, mybir.dt.from_np(a.dtype), kind="ExternalInput").ap()
    args["out"] = nc.dram_tensor("out_0", (B, S, E), F32, kind="ExternalOutput").ap()
    build(nc, **args)
    r = _run(nc, [arrays], core_ids=[0])
    return r.results[0]["out_0"]
```
